# Optimizing a Trainium2 kernel written in Bass

```python
import numpy as np
import jax
import jax.numpy as jnp

def _softmax(x, axis=-1):
    return jax.nn.softmax(x, axis=axis)

def _gelu(x):
    return jax.nn.gelu(x, approximate=True)

def _silu(x):
    return jax.nn.silu(x)

def _sigmoid(x):
    return jax.nn.sigmoid(x)

def _layernorm(x, axis=-1, eps=1e-05):
    m = jnp.mean(x, axis=axis, keepdims=True)
    v = jnp.var(x, axis=axis, keepdims=True)
    return (x - m) / jnp.sqrt(v + eps)

def _scatter_add(tgt, idx, src, axis=0):
    return tgt.at[idx].add(src)

def _segment_sum(src, seg, n):
    return jax.ops.segment_sum(src, seg, n)
kernel_name = 'mk_adaln_ffn_d1_seqx_r2_c54201'

def setup_inputs(seed: int=0):
    np.random.seed(seed)
    _w = jnp.asarray

    def _rec_inputs():
        import jax
        import jax.numpy as jnp
        _rk = jax.random.key(seed)
        x = -0.000125 + 0.9999 * jax.random.normal(jax.random.fold_in(_rk, 1), (8, 512, 1024), jnp.float32)
        _lenS = 512 - jax.random.randint(jax.random.fold_in(_rk, 7), (8,), 0, max(1, 512 // 4) + 1, jnp.int32)
        _lenS2 = 512 - jax.random.randint(jax.random.fold_in(_rk, 8), (8,), 0, max(1, 512 // 4) + 1, jnp.int32)
        cond_2048 = 0.000782532 + 0.100527 * jax.random.normal(jax.random.fold_in(_rk, 11), (8, 1024), jnp.float32)
        return (x, cond_2048)
    x, cond_2048 = _rec_inputs()

    def _L0_cond_setup():
        import jax, jax.numpy as jnp
        import numpy as np
        key = jax.random.key(seed)
        k1, k2, k3 = jax.random.split(key, 3)
        B, L, D, K = (4, 2048, 1024, 4)
        x = jax.random.normal(k1, (B, L, D), dtype=jnp.float32)
        w = jax.random.normal(k2, (K, 1, D), dtype=jnp.float32) * 0.1
        b = jax.random.normal(k3, (D,), dtype=jnp.float32) * 0.1
        return {'x': x, 'w': w, 'b': b}
    _L0_cond_all = _L0_cond_setup()
    _L0_cond_in = {k: v for k, v in _L0_cond_all.items() if k in ('b',)}
    del _L0_cond_all

    def _L0_ffn_setup():
        import jax, jax.numpy as jnp
        import numpy as np
        B, S, H, E = (2, 2048, 1024, 8)
        key = jax.random.key(seed)
        k1, k2, k3 = jax.random.split(key, 3)
        x = jax.random.normal(k1, (B, S, H), dtype=jnp.float32)
        w_router = jax.random.normal(k2, (E, H), dtype=jnp.float32) * (1.0 / np.sqrt(H))
        w_experts = jax.random.normal(k3, (E, H, H), dtype=jnp.float32) * (1.0 / np.sqrt(H))
        return {'x': x, 'w_router': w_router, 'w_experts': w_experts}
    _L0_ffn_all = _L0_ffn_setup()
    _L0_ffn_in = {k: v for k, v in _L0_ffn_all.items() if k in ('w_router', 'w_experts')}
    del _L0_ffn_all
    return {'x': x, 'cond_2048': cond_2048, 'L0_cond_b': _L0_cond_in['b'], 'L0_ffn_w_router': _L0_ffn_in['w_router'], 'L0_ffn_w_experts': _L0_ffn_in['w_experts']}

def reference(x, cond_2048, L0_cond_b, L0_ffn_w_router, L0_ffn_w_experts):
    import jax
    import jax.numpy as jnp

    def _L0_cond_ref(x, w, b):
        import jax, jax.numpy as jnp
        import numpy as np
        'Depthwise causal conv1d, channel-last.\n            x: (B, L, D); w: (K, 1, D); b: (D,). Returns (B, L, D).\n            Matches torch: Conv1d(D, D, K, groups=D, padding=K-1)(x.T)[..., :L].T\n            which is exactly a causal conv (left pad K-1, trim to L).\n            '
        K = w.shape[0]
        D = x.shape[-1]
        y = jax.lax.conv_general_dilated(x, w, window_strides=(1,), padding=[(K - 1, 0)], feature_group_count=D, dimension_numbers=('NWC', 'WIO', 'NWC'))
        return y + b

    def _L0_ffn_ref(x, w_router, w_experts):
        import jax, jax.numpy as jnp
        import numpy as np
        B, S, H, E = (2, 2048, 1024, 8)
        logits = jnp.einsum('bsh,eh->bse', x, w_router)
        idx = jnp.argmax(logits, axis=-1)
        all_out = jnp.einsum('bsh,efh->bsef', x, w_experts)
        out = jnp.take_along_axis(all_out, idx[:, :, None, None], axis=2)[:, :, 0, :]
        return out
    x = x + _L0_ffn_ref(_L0_cond_ref(x, cond_2048[:, None, :], L0_cond_b), L0_ffn_w_router, L0_ffn_w_experts)
    return x

_drawn_inputs = setup_inputs


def setup_inputs(seed=0):
    import zlib

    import numpy as np

    out = dict(_drawn_inputs(seed))
    spreads = {}
    factors = {}
    for name, (base, spread) in spreads.items():
        noise = np.random.default_rng([zlib.crc32(name.encode()), seed]).standard_normal(out[name].shape)
        drawn = base * np.exp(spread * noise) if base else spread * noise
        out[name] = jnp.asarray(drawn.astype(out[name].dtype))
    for name, factor in factors.items():
        out[name] = (out[name] * factor).astype(out[name].dtype)
    return out
```

```python
from contextlib import ExitStack

import numpy as np
import concourse.bass as bass
from concourse import mybir

ALU = mybir.AluOpType
ACT = mybir.ActivationFunctionType
AX = mybir.AxisListType
F32 = mybir.dt.float32
BF16 = mybir.dt.bfloat16
I32 = mybir.dt.int32
U32 = mybir.dt.uint32

P = 128
BATCH, SEQ, H, TAPS, EXPERTS = 8, 512, 1024, 8, 8
TOKENS = BATCH * SEQ
HC = H // P
TILES = TOKENS // P
TPB = SEQ // P
PAD = TAPS - 1
HALF = 512
SLOTS = (TOKENS + EXPERTS * (P - 1)) // P
RING = 3
ROUNDS = SLOTS // RING
assert ROUNDS * RING == SLOTS
WBUFS = 2

PE_TAPS = [list(range(3 if c % 2 == 0 else 2)) for c in range(HC)]
DVE_TAPS = [[k for k in range(TAPS) if k not in PE_TAPS[c]] for c in range(HC)]
N_DIAG = max(len(t) for t in PE_TAPS)
CONV_BANKS = 3

C_IDENT, C_BEFORE, C_ONES, C_IOTA = 0, P, 2 * P, 3 * P
C_FIRST = 4 * P
C_SLOT = C_FIRST + EXPERTS
C_TILE = C_SLOT + SLOTS
C_ROW = C_TILE + TILES
C_SPLIT = C_ROW + 1
N_CONST = C_SPLIT + TILES


def shape_constants():
    c = np.zeros((P, N_CONST), np.float32)
    c[:, C_IDENT:C_IDENT + P] = np.eye(P)
    c[:, C_BEFORE:C_BEFORE + P] = np.triu(np.ones((P, P)), 1)
    c[:, C_ONES:C_ONES + P] = 1.0
    c[:, C_IOTA:C_IOTA + P] = np.arange(P)
    c[:, C_FIRST:C_FIRST + EXPERTS] = EXPERTS - np.arange(EXPERTS)
    c[:, C_SLOT:C_SLOT + SLOTS] = np.arange(SLOTS)
    c[:, C_TILE:C_TILE + TILES] = np.arange(TILES) + 1
    c[:, C_ROW] = np.arange(P)
    c[:, C_SPLIT:C_SPLIT + TILES] = P * np.arange(TILES)
    return c


def dve_schedule():
    order, last, done = [], {}, {}
    for c in range(0, HC, 2):
        for n in range(max(len(DVE_TAPS[c]), len(DVE_TAPS[c + 1]))):
            for cc in (c, c + 1):
                if n < len(DVE_TAPS[cc]):
                    order.append((cc, DVE_TAPS[cc][n], last.get(cc)))
                    last[cc] = len(order) - 1
                    done[cc] = len(order)
    return order, done


DVE_ORDER, DVE_DONE = dve_schedule()
DVE_PER_BATCH = len(DVE_ORDER)


def build(nc, x_t, x_rows, conv_w, conv_b, router, experts, consts, out):
    ctx = ExitStack()
    with ctx:
        def sb(name, shape, dt=F32):
            return ctx.enter_context(nc.sbuf_tensor(name, shape, dt))

        def sem(name):
            return ctx.enter_context(nc.semaphore(name))

        y_dram = nc.dram_tensor("y_dram", [TOKENS, H], F32, kind="Internal").ap()

        cst = sb("cst", [P, N_CONST])
        taps = sb("taps", [P, HC, TAPS])
        bias = sb("bias", [P, HC])
        wr = sb("wr", [P, HC, EXPERTS])
        diag = sb("diag", [P, HC, N_DIAG, P])
        x_sb = sb("x_sb", [P, 2, HC, PAD + SEQ])
        y_t = sb("y_t", [P, 2, HC, SEQ])
        y_row = sb("y_row", [P, RING, H])
        x_row = sb("x_row", [P, RING, H])
        ys_t = sb("ys_t", [P, RING, HC, P])
        w_sb = sb("w_sb", [P, WBUFS, HC, H])
        logits = sb("logits", [P, TILES, EXPERTS])
        top = sb("top", [P, TILES])
        pick = sb("pick", [P, TILES, EXPERTS])
        chosen = sb("chosen", [P, TILES, EXPERTS])
        scan = sb("scan", [P, 2, TILES, EXPERTS])
        small = sb("small", [P, 6, EXPERTS])
        many = sb("many", [P, EXPERTS, TILES])
        pos = sb("pos", [P, TILES])
        pos_i = sb("pos_i", [P, 3, TILES], I32)
        slot_cmp = sb("slot_cmp", [P, SLOTS, EXPERTS])
        slot_f = sb("slot_f", [P, SLOTS])
        slot_expert = sb("slot_expert", [P, SLOTS], I32)
        slot_end = sb("slot_end", [P, EXPERTS], I32)
        ids = sb("ids", [P, 4, SLOTS])
        ids_i = sb("ids_i", [P, SLOTS], I32)
        idx = sb("idx", [P, RING], I32)

        ident = cst[:, C_IDENT:C_IDENT + P]
        x_flat = x_sb[:, :, :, :].rearrange("p a c s -> p (a c s)")
        nA, nB = TILES * P // 2, TILES * SLOTS
        row_hot = x_flat[:, 0:nA].bitcast(BF16).rearrange("p (t r) -> p t r", t=TILES)
        slot_hot = x_flat[:, nA:nA + nB].bitcast(BF16).rearrange("p (t s) -> p t s", t=TILES)
        slot_eq = x_flat[:, nA + nB:nA + 2 * nB].rearrange("p (t s) -> p t s", t=TILES)

        ps = ctx.enter_context(nc.psum_tensor("ps", [P, 8, HALF], F32))
        conv_ps = [ps[:, n, :] for n in range(CONV_BANKS)]
        logit_ps = ps[:, 3, 0:TILES * EXPERTS].rearrange("p (t e) -> p t e", t=TILES)
        rank_ps = ps[:, 4, 0:TILES * EXPERTS].rearrange("p (t e) -> p t e", t=TILES)
        total_ps = ps[:, 5, 0:TILES * EXPERTS].rearrange("p (t e) -> p t e", t=TILES)
        ids_ps = ps[:, 3, 0:2 * SLOTS]
        turn_ps = [ps[:, 6 + h, :] for h in range(2)]
        out_ps = [ps[:, 2 * k:2 * k + 2, :].rearrange("p a n -> p (a n)") for k in range(RING)]

        const_in = sem("const_in")
        diag_ready = sem("diag_ready")
        pads_zero = sem("pads_zero")
        rows_zero = sem("rows_zero")
        x_in = [sem(f"x_in{n}") for n in range(2)]
        conv_mm = sem("conv_mm")
        conv_seed = sem("conv_seed")
        taps_done = sem("taps_done")
        turned = sem("turned")
        turn_copied = sem("turn_copied")
        logit_done = sem("logit_done")
        y_out = [sem(f"y_out{n}") for n in range(2)]
        route_step = sem("route_step")
        chosen_ready = sem("chosen_ready")
        ranked = sem("ranked")
        hot_ready = sem("hot_ready")
        ids_done = sem("ids_done")
        slots_ready = sem("slots_ready")
        ids_ready = sem("ids_ready")
        w_in = [sem(f"w_in{n}") for n in range(WBUFS)]
        w_ready = sem("w_ready")
        idx_ready = sem("idx_ready")
        gather_issued = sem("gather_issued")
        scatter_issued = sem("scatter_issued")
        y_got = [sem(f"y_got{n}") for n in range(RING)]
        x_got = [sem(f"x_got{n}") for n in range(RING)]
        ys_turned = sem("ys_turned")
        ys_ready = sem("ys_ready")
        gemm_done = sem("gemm_done")
        res_done = sem("res_done")
        row_out = [sem(f"row_out{n}") for n in range(RING)]

        block = ctx.enter_context(nc.Block())
        PAIRS = BATCH // 2

        @block.sync
        def _(sp):
            for dst, src in ((cst[:, :], consts), (taps[:, :, :], conv_w), (bias[:, :], conv_b),
                             (wr[:, :, :], router)):
                sp.dma_start(dst, src).then_inc(const_in, 16)

            def load_x(b, n):
                sp.dma_start(x_sb[:, n, :, PAD:], x_t[bass.ds(b, 1)].rearrange("b p c s -> (b p) c s")
                             if not isinstance(b, int) else x_t[b]).then_inc(x_in[n], 16)

            def store_y(b, n):
                for j in range(TPB):
                    sp.wait_ge(turn_copied, (b * TPB + j + 1) * 2)
                    sp.dma_start(y_dram[bass.ds((b * TPB + j) * P, P), :], y_row[:, j % 2, :]).then_inc(y_out[j % 2], 16)

            load_x(0, 0)
            load_x(1, 1)
            for e in range(WBUFS):
                sp.dma_start(w_sb[:, e], experts[e]).then_inc(w_in[e], 16)
            with sp.Fori(0, PAIRS - 1) as i:
                for n in range(2):
                    sp.wait_ge(taps_done, (i * 2 + n + 1) * DVE_PER_BATCH)
                    load_x(i * 2 + n + 2, n)
                    store_y(i * 2 + n, n)
            for n in range(2):
                store_y(BATCH - 2 + n, n)
            for e in range(WBUFS):
                sp.wait_ge(w_in[e], 16)
                sp.sem_inc(w_ready, 1)
            sp.wait_ge(slots_ready, 1)
            with sp.Fori(1, EXPERTS // WBUFS) as i:
                for n in range(WBUFS):
                    end = sp.value_load(slot_end[0:1, bass.ds(i * WBUFS + n - WBUFS, 1)], min_val=0, max_val=SLOTS)
                    sp.wait_ge(gemm_done, end)
                    sp.dma_start(w_sb[:, n], experts[bass.ds(i * WBUFS + n, 1)].rearrange("e p c f -> (e p) c f")
                                 ).then_inc(w_in[n], 16)
                    sp.wait_ge(w_in[n], (i + 1) * 16)
                    sp.sem_inc(w_ready, 1)

        @block.scalar
        def _(act):
            act.wait_ge(const_in, 64)

            def batch(b, n, first):
                for c in range(HC):
                    act.wait_ge(conv_mm, b * HC + c + 1)
                    if not first:
                        act.wait_ge(logit_done, (b - 1) * TPB)
                    nc.scalar.activation(y_t[:, n, c, :], conv_ps[c % CONV_BANKS] if isinstance(b, int) else
                                         conv_bank(b, c), ACT.Identity, bias=bias[:, c:c + 1]).then_inc(conv_seed, 1)

            def conv_bank(b, c):
                return conv_ps[c % CONV_BANKS]

            def rows(b, n, first):
                for j in range(TPB):
                    for h in range(2):
                        act.wait_ge(turned, (b * TPB + j) * 2 + h + 1)
                        if h == 0 and not (first and j < 2):
                            act.wait_ge(y_out[j % 2], ((b * TPB + j) // 2) * 16 if isinstance(b, int)
                                        else b * (TPB // 2 * 16) + (j // 2) * 16)
                        nc.scalar.copy(y_row[:, j % 2, h * HALF:(h + 1) * HALF], turn_ps[h]).then_inc(turn_copied, 1)

            batch(0, 0, True)
            batch(1, 1, True)
            rows(0, 0, True)
            with act.Fori(1, PAIRS) as i:
                batch(i * 2, 0, False)
                rows(i * 2 - 1, 1, False)
                batch(i * 2 + 1, 1, False)
                rows(i * 2, 0, False)
            rows(BATCH - 1, 1, False)

            def slot(i, k, first):
                for h in range(2):
                    act.wait_ge(ys_turned, (i * RING + k) * 2 + h + 1)
                    if not first:
                        act.wait_ge(gemm_done, i * RING + (k + 1 - RING))
                    nc.scalar.copy(ys_t[:, k, 4 * h:4 * h + 4, :].rearrange("p c s -> p (c s)"), turn_ps[h]
                                   ).then_inc(ys_ready, 1)

            for k in range(RING):
                slot(0, k, True)
            with act.Fori(1, ROUNDS) as i:
                for k in range(RING):
                    slot(i, k, False)

        @block.vector
        def _(dve):
            for n in range(2):
                nc.vector.memset(x_sb[:, n, :, 0:PAD], 0.0).then_inc(pads_zero, 1)
            nc.vector.memset(y_row[:, 2, :], 0.0).then_inc(rows_zero, 1)
            nc.vector.memset(x_row[:, :, :], 0.0).then_inc(rows_zero, 1)
            dve.wait_ge(const_in, 64)
            dve.wait_ge(pads_zero, 2)

            def batch(b, n, half):
                dve.wait_ge(x_in[n], (half + 1) * 16)
                for m, (c, k, before) in enumerate(DVE_ORDER):
                    if before is None:
                        dve.wait_ge(conv_seed, b * HC + c + 1)
                    else:
                        dve.wait_ge(taps_done, b * DVE_PER_BATCH + before + 1)
                    y = y_t[:, n, c, :]
                    nc.vector.scalar_tensor_tensor(out=y, in0=x_sb[:, n, c, k:k + SEQ], scalar=taps[:, c, k:k + 1],
                                                   in1=y, op0=ALU.mult, op1=ALU.add).then_inc(taps_done, 1)

            with dve.Fori(0, PAIRS) as i:
                for n in range(2):
                    batch(i * 2 + n, n, i)

            steps = [0]

            def step(ins):
                steps[0] += 1
                ins.then_inc(route_step, 1)
                dve.wait_ge(route_step, steps[0])

            def per_token(a):
                return a.unsqueeze(2).to_broadcast([P, TILES, EXPERTS])

            def per_tile(a):
                return a.unsqueeze(1).to_broadcast([P, TILES, EXPERTS])

            dve.wait_ge(logit_done, TILES)
            step(nc.vector.tensor_copy(logits[:, :, :], logit_ps))
            step(nc.vector.tensor_reduce(top[:, :], logits[:, :, :], AX.X, ALU.max))
            step(nc.vector.tensor_tensor(pick[:, :, :], logits[:, :, :], per_token(top[:, :]), ALU.is_equal))
            step(nc.vector.tensor_tensor(pick[:, :, :], pick[:, :, :], per_tile(cst[:, C_FIRST:C_FIRST + EXPERTS]), ALU.mult))
            step(nc.vector.tensor_reduce(top[:, :], pick[:, :, :], AX.X, ALU.max))
            step(nc.vector.tensor_scalar(top[:, :], top[:, :], 1.0, None, ALU.max))
            nc.vector.tensor_tensor(chosen[:, :, :], per_token(top[:, :]), per_tile(cst[:, C_FIRST:C_FIRST + EXPERTS]),
                                    ALU.is_equal).then_inc(chosen_ready, 1)

            dve.wait_ge(ranked, 1)
            step(nc.vector.tensor_copy(scan[:, 0], total_ps))
            src = 0
            d = 1
            while d < TILES:
                nc.vector.tensor_copy(scan[:, 1 - src, 0:d], scan[:, src, 0:d]).then_inc(route_step, 1)
                steps[0] += 1
                step(nc.vector.tensor_tensor(scan[:, 1 - src, d:], scan[:, src, d:], scan[:, src, :TILES - d], ALU.add))
                src, d = 1 - src, 2 * d
            count = scan[:, src, TILES - 1]
            step(nc.vector.tensor_tensor(many[:, :, :], count.unsqueeze(2).to_broadcast([P, EXPERTS, TILES]),
                                         cst[:, C_SPLIT:C_SPLIT + TILES].unsqueeze(1).to_broadcast([P, EXPERTS, TILES]),
                                         ALU.is_gt))
            step(nc.vector.tensor_reduce(small[:, 0, :], many[:, :, :], AX.X, ALU.add))
            step(nc.vector.tensor_scalar(small[:, 0, :], small[:, 0, :], 1.0, None, ALU.max))
            ends, d = 0, 1
            while d < EXPERTS:
                nc.vector.tensor_copy(small[:, 1 - ends, 0:d], small[:, ends, 0:d]).then_inc(route_step, 1)
                steps[0] += 1
                if d == 1:
                    nc.vector.tensor_copy(small[:, 2, :], small[:, ends, :]).then_inc(route_step, 1)
                    steps[0] += 1
                step(nc.vector.tensor_tensor(small[:, 1 - ends, d:], small[:, ends, d:], small[:, ends, :EXPERTS - d], ALU.add))
                ends, d = 1 - ends, 2 * d
            end = small[:, ends, :]
            step(nc.vector.tensor_tensor(small[:, 3, :], end, small[:, 2, :], ALU.subtract))
            step(nc.vector.tensor_scalar(small[:, 4, :], small[:, 3, :], float(P), None, ALU.mult))
            step(nc.vector.tensor_tensor(pick[:, :, :], rank_ps, per_tile(small[:, 4, :]), ALU.add))
            step(nc.vector.tensor_tensor(pick[:, 1:, :], pick[:, 1:, :], scan[:, src, :TILES - 1], ALU.add))
            step(nc.vector.tensor_tensor(pick[:, :, :], pick[:, :, :], chosen[:, :, :], ALU.mult))
            step(nc.vector.tensor_reduce(pos[:, :], pick[:, :, :], AX.X, ALU.add))
            step(nc.vector.tensor_copy(pos_i[:, 0, :], pos[:, :]))
            step(nc.vector.tensor_scalar(pos_i[:, 1, :], pos_i[:, 0, :], P - 1, None, ALU.bitwise_and))
            step(nc.vector.tensor_scalar(pos_i[:, 2, :], pos_i[:, 0, :], 7, None, ALU.logical_shift_right))
            step(nc.vector.tensor_tensor(row_hot, pos_i[:, 1, :].unsqueeze(2).to_broadcast([P, TILES, P]),
                                         cst[:, C_IOTA:C_IOTA + P].unsqueeze(1).to_broadcast([P, TILES, P]), ALU.is_equal))
            step(nc.vector.tensor_tensor(slot_eq, pos_i[:, 2, :].unsqueeze(2).to_broadcast([P, TILES, SLOTS]),
                                         cst[:, C_SLOT:C_SLOT + SLOTS].unsqueeze(1).to_broadcast([P, TILES, SLOTS]),
                                         ALU.is_equal))
            nc.vector.tensor_scalar(slot_hot[:, :, 0:SLOTS], slot_eq, cst[:, C_ROW:C_ROW + 1], None, ALU.mult
                                    ).then_inc(hot_ready, 1)
            nc.vector.tensor_tensor(slot_hot[:, :, SLOTS:], slot_eq,
                                    cst[:, C_TILE:C_TILE + TILES].unsqueeze(2).to_broadcast([P, TILES, SLOTS]),
                                    ALU.mult).then_inc(hot_ready, 1)
            step(nc.vector.tensor_tensor(slot_cmp[:, :, :], cst[:, C_SLOT:C_SLOT + SLOTS].unsqueeze(2).to_broadcast([P, SLOTS, EXPERTS]),
                                         end.unsqueeze(1).to_broadcast([P, SLOTS, EXPERTS]), ALU.is_ge))
            step(nc.vector.tensor_reduce(slot_f[:, :], slot_cmp[:, :, :], AX.X, ALU.add))
            step(nc.vector.tensor_scalar(slot_expert[:, :], slot_f[:, :], float(EXPERTS - 1), None, ALU.min))
            nc.vector.tensor_copy(slot_end[:, :], end).then_inc(slots_ready, 1)
            dve.wait_ge(ids_done, 1)
            step(nc.vector.tensor_copy(ids[:, 0:2, :].rearrange("p a s -> p (a s)"), ids_ps))
            step(nc.vector.tensor_scalar(ids[:, 2, :], ids[:, 1, :], 0.5, float(2 * TOKENS), ALU.is_lt, ALU.mult))
            step(nc.vector.scalar_tensor_tensor(out=ids[:, 3, :], in0=ids[:, 1, :], scalar=float(P), in1=ids[:, 0, :],
                                                op0=ALU.mult, op1=ALU.add))
            nc.vector.scalar_tensor_tensor(out=ids_i[:, :], in0=ids[:, 3, :], scalar=float(-P), in1=ids[:, 2, :],
                                           op0=ALU.add, op1=ALU.add).then_inc(ids_ready, 1)

            def slot(i, k):
                dve.wait_ge(gemm_done, i * RING + k + 1)
                dve.wait_ge(x_got[k], (i + 1) * 16)
                nc.vector.tensor_tensor(x_row[:, k, :], out_ps[k], x_row[:, k, :], ALU.add).then_inc(res_done, 1)

            with dve.Fori(0, ROUNDS) as i:
                for k in range(RING):
                    slot(i, k)

        @block.tensor
        def _(pe):
            pe.wait_ge(const_in, 64)
            pe.wait_ge(diag_ready, sum(len(t) for t in PE_TAPS))
            pe.wait_ge(pads_zero, 2)

            def conv(b, n, half, first):
                pe.wait_ge(x_in[n], (half + 1) * 16)
                for c in range(HC):
                    if not (first and c < CONV_BANKS):
                        prev = c - CONV_BANKS if c >= CONV_BANKS else (c + HC - 1 - (HC - 1 - c) % CONV_BANKS) - HC
                        back = max(m for m in range(HC) if m % CONV_BANKS == c % CONV_BANKS) - HC if c < CONV_BANKS else c - CONV_BANKS
                        pe.wait_ge(conv_seed, b * HC + back + 1)
                    for k in PE_TAPS[c]:
                        mm = nc.tensor.matmul(conv_ps[c % CONV_BANKS], diag[:, c, k, :], x_sb[:, n, c, k:k + SEQ],
                                              start=(k == PE_TAPS[c][0]), stop=(k == PE_TAPS[c][-1]))
                    mm.then_inc(conv_mm, 1)

            def post(b, n, first):
                pe.wait_ge(taps_done, (b + 1) * DVE_PER_BATCH)
                for j in range(TPB):
                    cols = slice(j * P, (j + 1) * P)
                    for h in range(2):
                        if not (first and j == 0):
                            pe.wait_ge(turn_copied, (b * TPB + j) * 2 + h - 1)
                        for q in range(4):
                            tr = nc.tensor.transpose(turn_ps[h][:, q * P:(q + 1) * P], y_t[:, n, 4 * h + q, cols], ident)
                        tr.then_inc(turned, 1)
                    for c in range(HC):
                        mm = nc.tensor.matmul(logit_tile(b, j), y_t[:, n, c, cols], wr[:, c, :],
                                              start=(c == 0), stop=(c == HC - 1))
                    mm.then_inc(logit_done, 1)

            def logit_tile(b, j):
                return ps[:, 3, bass.ds((b * TPB + j) * EXPERTS, EXPERTS)]

            conv(0, 0, 0, True)
            conv(1, 1, 0, False)
            post(0, 0, True)
            with pe.Fori(1, PAIRS) as i:
                conv(i * 2, 0, i, False)
                post(i * 2 - 1, 1, False)
                conv(i * 2 + 1, 1, i, False)
                post(i * 2, 0, False)
            post(BATCH - 1, 1, False)

            pe.wait_ge(chosen_ready, 1)
            hot = chosen[:, :, :].rearrange("p t e -> p (t e)")
            nc.tensor.matmul(ps[:, 4, 0:TILES * EXPERTS], cst[:, C_BEFORE:C_BEFORE + P], hot, start=True, stop=True)
            nc.tensor.matmul(ps[:, 5, 0:TILES * EXPERTS], cst[:, C_ONES:C_ONES + P], hot, start=True, stop=True
                             ).then_inc(ranked, 1)
            pe.wait_ge(hot_ready, 2)
            for t in range(TILES):
                mm = nc.tensor.matmul(ids_ps, row_hot[:, t, :], slot_hot[:, t, :], start=(t == 0), stop=(t == TILES - 1))
            mm.then_inc(ids_done, 1)

            def turn(i, k, first):
                pe.wait_ge(y_got[k], (i + 1) * 16)
                for h in range(2):
                    if not first:
                        pe.wait_ge(ys_ready, (i * RING + k) * 2 + (h - 1))
                    for q in range(4):
                        c = 4 * h + q
                        tr = nc.tensor.transpose(turn_ps[h][:, q * P:(q + 1) * P], y_row[:, k, c * P:(c + 1) * P], ident)
                    tr.then_inc(ys_turned, 1)

            def gemm(i, k, first):
                e = pe.value_load(slot_expert[0:1, bass.ds(i * RING + k, 1)] if not isinstance(i, int)
                                  else slot_expert[0:1, i * RING + k:i * RING + k + 1], min_val=0, max_val=EXPERTS - 1)
                pe.wait_ge(ys_ready, (i * RING + k) * 2 + 2)
                pe.wait_ge(w_ready, e + 1)
                if not first:
                    pe.wait_ge(res_done, i * RING + (k + 1 - RING))
                buf = e % WBUFS
                w_flat = w_sb[:, :, :, :].rearrange("p b c f -> p (b c f)")
                for c in range(HC):
                    for f in range(2):
                        mm = nc.tensor.matmul(out_ps[k][:, f * HALF:(f + 1) * HALF], ys_t[:, k, c, :],
                                              w_flat[:, bass.ds(buf * (HC * H) + (c * H + f * HALF), HALF)],
                                              start=(c == 0), stop=(c == HC - 1))
                mm.then_inc(gemm_done, 1)

            pe.wait_ge(slots_ready, 1)
            pe.wait_ge(rows_zero, 2)
            turn(0, 0, True)
            for k in range(RING):
                turn((k + 1) // RING, (k + 1) % RING, False)
                gemm(0, k, True)
            with pe.Fori(1, ROUNDS - 1) as i:
                for k in range(RING):
                    turn(i + (k + 1) // RING, (k + 1) % RING, False)
                    gemm(i, k, False)
            for k in range(RING):
                if k + 1 < RING:
                    turn(ROUNDS - 1, k + 1, False)
                gemm(ROUNDS - 1, k, False)

        @block.gpsimd
        def _(pool):
            last_token = pool.alloc_register("last_token")
            pool.wait_ge(const_in, 64)
            for c in range(HC):
                for k in PE_TAPS[c]:
                    nc.gpsimd.tensor_scalar(diag[:, c, k, :], ident, taps[:, c, k:k + 1], None, ALU.mult
                                            ).then_inc(diag_ready, 1)

            def gather(i, k, first):
                if not first:
                    pool.wait_ge(row_out[k], i * 16)
                    pool.wait_ge(ys_turned, (i * RING + k) * 2 + (2 - 2 * RING))
                nc.gpsimd.tensor_copy(idx[:, k:k + 1], ids_i[:, bass.ds(i * RING + k, 1)]).then_inc(idx_ready, 1)
                pool.wait_ge(idx_ready, i * RING + k + 1)
                pool.sem_inc(gather_issued, 1)
                at = bass.IndirectOffsetOnAxis(ap=idx[:, k:k + 1].bitcast(U32), axis=0)
                nc.gpsimd.indirect_dma_start(y_row[:, k, :], None, y_dram, at, bounds_check=last_token,
                                             oob_is_err=False).then_inc(y_got[k], 16)
                nc.gpsimd.indirect_dma_start(x_row[:, k, :], None, x_rows, at, bounds_check=last_token,
                                             oob_is_err=False).then_inc(x_got[k], 16)

            def scatter(i, k):
                pool.wait_ge(res_done, i * RING + k + 1)
                pool.sem_inc(scatter_issued, 1)
                at = bass.IndirectOffsetOnAxis(ap=idx[:, k:k + 1].bitcast(U32), axis=0)
                nc.gpsimd.indirect_dma_start(out, at, x_row[:, k, :], None, bounds_check=last_token,
                                             oob_is_err=False).then_inc(row_out[k], 16)

            pool.reg_mov(last_token, TOKENS - 1)
            pool.wait_ge(y_out[0], 16 * TILES // 2)
            pool.wait_ge(y_out[1], 16 * TILES // 2)
            pool.wait_ge(rows_zero, 2)
            pool.wait_ge(ids_ready, 1)
            gather(0, 0, True)
            gather(0, 1, True)
            gather(0, 2, True)
            scatter(0, 0)
            with pool.Fori(1, ROUNDS) as i:
                gather(i, 0, False)
                scatter(i - 1, 1)
                gather(i, 1, False)
                scatter(i - 1, 2)
                gather(i, 2, False)
                scatter(i, 0)
            scatter(ROUNDS - 1, 1)
            scatter(ROUNDS - 1, 2)
            for k in range(RING):
                pool.wait_ge(row_out[k], 16 * ROUNDS)


def kernel(x, cond_2048, L0_cond_b, L0_ffn_w_router, L0_ffn_w_experts):
    import numpy as _np
    import concourse.bacc as _bacc
    from concourse import mybir as _mybir
    from concourse.bass_utils import run_bass_kernel_spmd as _run

    x = _np.asarray(x)
    arrays = {
        "x_t": x.reshape(BATCH, SEQ, HC, P).transpose(0, 3, 2, 1),
        "x_rows": x.reshape(TOKENS, H),
        "conv_w": _np.asarray(cond_2048).reshape(TAPS, HC, P).transpose(2, 1, 0),
        "conv_b": _np.asarray(L0_cond_b).reshape(HC, P).transpose(1, 0),
        "router": _np.asarray(L0_ffn_w_router).reshape(EXPERTS, HC, P).transpose(2, 1, 0),
        "experts": _np.asarray(L0_ffn_w_experts).reshape(EXPERTS, H, HC, P).transpose(0, 3, 2, 1),
        "consts": shape_constants(),
    }
    arrays = {k: _np.ascontiguousarray(v) for k, v in arrays.items()}
    nc = _bacc.Bacc("TRN2", target_bir_lowering=False, num_devices=1)
    args = [nc.dram_tensor(k, v.shape, _mybir.dt.from_np(v.dtype), kind="ExternalInput").ap() for k, v in arrays.items()]
    out = nc.dram_tensor("out", (TOKENS, H), _mybir.dt.float32, kind="ExternalOutput").ap()
    build(nc, *args, out)
    r = _run(nc, [arrays], core_ids=[0])
    return r.results[0]["out"].reshape(BATCH, SEQ, H)
```

```python
from contextlib import ExitStack

import numpy as np
import concourse.bass as bass
from concourse import mybir

ALU = mybir.AluOpType
ACT = mybir.ActivationFunctionType
AX = mybir.AxisListType
F32 = mybir.dt.float32
F32R = mybir.dt.float32r
BF16 = mybir.dt.bfloat16
I32 = mybir.dt.int32
U32 = mybir.dt.uint32

P = 128
BATCH, SEQ, H, TAPS, EXPERTS = 8, 512, 1024, 8, 8
TOKENS = BATCH * SEQ
HC = H // P
TILES = TOKENS // P
PAD = TAPS - 1
HALF = 512
GROUP = 2
GROUPS = BATCH // GROUP
TPG = GROUP * SEQ // P
MOST_SLOTS = (TOKENS + EXPERTS * (P - 1)) // P
RING = 2
ROUNDS = -(-MOST_SLOTS // RING)
SLOTS = ROUNDS * RING + 1
HI, LO = 0, 1
WBUFS = 2
RAW = HC
W_SIZE = 2 * HC * H

PE_COUNT = [0, 0, 5, 4, 0, 0, 5, 4]
PE_TAPS = [list(range(n)) for n in PE_COUNT]
ACT_TAP = TAPS - 1
DVE_TAPS = [[k for k in range(TAPS) if k >= n and (n or k != ACT_TAP)] for n in PE_COUNT]
PE_CHUNKS = [c for c in range(HC) if PE_COUNT[c]]
N_PE = len(PE_CHUNKS)
assert N_PE % 2 == 0
DIAG = {ck: n for n, ck in enumerate((c, k) for c in range(HC) for k in PE_TAPS[c])}
LAG = 4

C_IDENT, C_BEFORE, C_ONES, C_IOTA = 0, P, 2 * P, 3 * P
C_FIRST = 4 * P
C_SLOT = C_FIRST + EXPERTS
C_TILE = C_SLOT + SLOTS
C_ROW = C_TILE + TILES
C_SPLIT = C_ROW + 1
C_CARRY = C_SPLIT + TILES
N_CONST = C_CARRY + EXPERTS * TILES


def shape_constants():
    c = np.zeros((P, N_CONST), np.float32)
    c[:, C_IDENT:C_IDENT + P] = np.eye(P)
    c[:, C_BEFORE:C_BEFORE + P] = np.triu(np.ones((P, P)), 1)
    c[:, C_ONES:C_ONES + P] = 1.0
    c[:, C_IOTA:C_IOTA + P] = np.arange(P)
    c[:, C_FIRST:C_FIRST + EXPERTS] = EXPERTS - np.arange(EXPERTS)
    c[:, C_SLOT:C_SLOT + SLOTS] = np.arange(SLOTS)
    c[:, C_TILE:C_TILE + TILES] = np.arange(TILES) + 1
    c[:, C_ROW] = np.arange(P)
    c[:, C_SPLIT:C_SPLIT + TILES] = P * np.arange(TILES)
    c[:, C_CARRY:C_CARRY + EXPERTS * TILES] = (np.arange(EXPERTS * TILES) % TILES > 0)
    return c


def dve_schedule():
    lanes = [[(c, k) for c in range(n, HC, 2) for k in DVE_TAPS[c]] for n in range(2)]
    order, last, done = [], {}, {}
    for n in range(max(map(len, lanes))):
        for lane in lanes:
            if n < len(lane):
                c, k = lane[n]
                order.append((c, k, last.get(c)))
                last[c] = len(order) - 1
                done[c] = len(order)
    return order, done


DVE_ORDER, DVE_DONE = dve_schedule()
DVE_PER_GROUP = len(DVE_ORDER)


def build(nc, x_t, x_rows, conv_w, conv_b, router, experts, consts, out):
    ctx = ExitStack()
    with ctx:
        def sb(name, shape, dt=F32):
            return ctx.enter_context(nc.sbuf_tensor(name, shape, dt))

        def sem(name):
            return ctx.enter_context(nc.semaphore(name))

        y_dram = nc.dram_tensor("y_dram", [TOKENS, H], F32, kind="Internal").ap()

        x_size, y_size = HC * GROUP * (PAD + SEQ), HC * GROUP * SEQ
        w_at = -(-nc.sbuf_base // 32) * 32
        w_all = sb("w_all", [P, max(WBUFS * W_SIZE, (WBUFS - 1) * W_SIZE + x_size + y_size)], F32R)
        assert nc.sbuf_base >= w_at + 4 * WBUFS * W_SIZE
        conv_at = w_at + 4 * (WBUFS - 1) * W_SIZE
        x_sb = nc.alloc_sbuf_tensor_at("x_sb", [P, HC, GROUP, PAD + SEQ], F32, offset=conv_at)
        y_t = nc.alloc_sbuf_tensor_at("y_t", [P, HC, GROUP, SEQ], F32, offset=conv_at + 4 * x_size)
        w_raw = sb("w_raw", [P, RAW, H])
        rows = sb("rows", [P, 2 * RING, H])
        y_row, x_row = rows[:, 0:RING, :], rows[:, RING:2 * RING, :]
        stage = [rows[:, 2 * n:2 * n + 2, :].rearrange("p a n -> p (a n)").rearrange("p (j n) -> p j n", j=TPG)
                 for n in range(2)]
        ys_at = -(-nc.sbuf_base // 32) * 32
        ys = sb("ys", [P, 2, RING, HC, P], F32R)
        assert len(DIAG) * P <= 2 * RING * HC * P and nc.sbuf_base >= ys_at + 4 * 2 * RING * HC * P
        diag = nc.alloc_sbuf_tensor_at("diag", [P, len(DIAG), P], F32, offset=ys_at)

        cst = sb("cst", [P, N_CONST])
        taps = sb("taps", [P, HC, TAPS])
        bias = sb("bias", [P, HC])
        wr = sb("wr", [P, HC, EXPERTS])
        logits = sb("logits", [P, TILES, EXPERTS])
        top = sb("top", [P, TILES])
        pick = sb("pick", [P, TILES, EXPERTS])
        place = sb("place", [P, EXPERTS, TILES])
        chosen = sb("chosen", [P, TILES, EXPERTS], BF16)
        before = sb("before", [P, 2 * P], BF16)
        scan = sb("scan", [P, EXPERTS, TILES])
        small = sb("small", [P, 6, EXPERTS])
        many = sb("many", [P, EXPERTS, TILES])
        pos = sb("pos", [P, TILES])
        pos_i = sb("pos_i", [P, 3, TILES], I32)
        slot_cmp = sb("slot_cmp", [P, SLOTS, EXPERTS])
        slot_f = sb("slot_f", [P, SLOTS])
        slot_expert = sb("slot_expert", [P, SLOTS], I32)
        slot_first = sb("slot_first", [P, SLOTS], I32)
        ids = sb("ids", [P, 4, SLOTS])
        ids_i = sb("ids_i", [P, SLOTS], I32)
        idx = sb("idx", [P, 2, RING], I32)
        last_round = sb("last_round", [P, 3], I32)
        full_rounds = sb("full_rounds", [P, 1], I32)

        w_sb = w_all[:, 0:WBUFS * W_SIZE]
        ident = cst[:, C_IDENT:C_IDENT + P]
        x_flat = x_sb[:, :, :, :].rearrange("p c b s -> p (c b s)")
        nA, nB = TILES * P // 2, TILES * SLOTS
        row_hot = x_flat[:, 0:nA].bitcast(BF16).rearrange("p (t r) -> p t r", t=TILES)
        slot_hot = x_flat[:, nA:nA + nB].bitcast(BF16).rearrange("p (t s) -> p t s", t=TILES)
        slot_eq = x_flat[:, nA + nB:nA + 2 * nB].rearrange("p (t s) -> p t s", t=TILES)

        ps = ctx.enter_context(nc.psum_tensor("ps", [P, 8, HALF], F32))
        conv_ps = [ps[:, 2 * n:2 * n + 2, :] for n in range(2)]
        logit_ps = ps[:, 4, 0:TILES * EXPERTS].rearrange("p (t e) -> p t e", t=TILES)
        rank_ps = ps[:, 0, 0:EXPERTS * TILES]
        total_ps = ps[:, 1, 0:EXPERTS * TILES]
        ids_ps = ps[:, 2, 0:2 * SLOTS]
        turn_ps = [ps[:, 6 + h, :] for h in range(2)]
        turn_both = ps[:, 6:8, :].rearrange("p a n -> p (a n)")
        out_ps = [ps[:, 2 * k:2 * k + 2, :].rearrange("p a n -> p (a n)") for k in range(RING)]

        taps_in = sem("taps_in")
        bias_in = sem("bias_in")
        ident_in = sem("ident_in")
        const_in = sem("const_in")
        router_in = sem("router_in")
        before_ready = sem("before_ready")
        diag_ready = sem("diag_ready")
        pads_zero = sem("pads_zero")
        x_in = [sem(f"x_in{c}") for c in range(HC)]
        conv_mm = sem("conv_mm")
        conv_seed = sem("conv_seed")
        taps_done = sem("taps_done")
        turned = sem("turned")
        turn_copied = sem("turn_copied")
        logit_done = sem("logit_done")
        y_out = [sem(f"y_out{n}") for n in range(2)]
        route_step = sem("route_step")
        chosen_ready = sem("chosen_ready")
        ranked = sem("ranked")
        slot_known = sem("slot_known")
        hot_ready = sem("hot_ready")
        row_hot_ready = sem("row_hot_ready")
        ids_done = sem("ids_done")
        slots_ready = sem("slots_ready")
        ids_ready = sem("ids_ready")
        raw_in = [sem(f"raw_in{n}") for n in range(RAW)]
        w_hi = sem("w_hi")
        w_split = sem("w_split")
        idx_ready = sem("idx_ready")
        dma_allowed = sem("dma_allowed")
        y_got = [sem(f"y_got{n}") for n in range(RING)]
        x_got = [sem(f"x_got{n}") for n in range(RING)]
        ys_turned = sem("ys_turned")
        ys_hi = sem("ys_hi")
        ys_lo = sem("ys_lo")
        gemm_done = sem("gemm_done")
        res_done = sem("res_done")
        row_out = [sem(f"row_out{n}") for n in range(RING)]

        block = ctx.enter_context(nc.Block())
        TURN_LATE = 2
        HOT = 8
        LOW_FIRST = 3
        HIGH_SECOND = 4

        def pe_units(g, c):
            return g * N_PE + sum(m <= c for m in PE_CHUNKS)

        @block.sync
        def _(sp):
            def load_x(g, c):
                src = x_t[g, c] if isinstance(g, int) else x_t[bass.ds(g, 1), c].rearrange("g p b s -> (g p) b s")
                sp.dma_start(x_sb[:, c, :, PAD:], src).then_inc(x_in[c], 16)

            def load_raw(e, c, first):
                if not first:
                    sp.wait_ge(w_split, e * HC + (c + 1 - RAW))
                src = (experts[e, :, c, :] if isinstance(e, int)
                       else experts[bass.ds(e, 1), :, c, :].rearrange("e p f -> (e p) f"))
                sp.dma_start(w_raw[:, c % RAW, :], src).then_inc(raw_in[c % RAW], 16)

            def store_y(g, m):
                sp.wait_ge(turn_copied, (g * HC + 2 * m + 2) * 2)
                sp.dma_start(y_dram[bass.ds(g * (TPG * P), TPG * P), 2 * m * P:(2 * m + 2) * P]
                             .rearrange("(j p) n -> p j n", p=P), stage[m % 2]).then_inc(y_out[m % 2], 16)

            sp.dma_start(taps[:, :, :], conv_w).then_inc(taps_in, 16)
            load_x(0, 0)
            sp.dma_start(bias[:, :], conv_b).then_inc(bias_in, 16)
            load_x(0, 1)
            sp.dma_start(ident, consts[:, C_IDENT:C_IDENT + P]).then_inc(ident_in, 16)
            load_x(0, PE_CHUNKS[0])
            sp.dma_start(wr[:, :, :], router).then_inc(router_in, 16)
            for c in range(2, HC):
                if c != PE_CHUNKS[0]:
                    load_x(0, c)
            sp.dma_start(cst[:, P:], consts[:, P:]).then_inc(const_in, 16)
            for c in range(HC):
                load_raw(0, c, True)
            with sp.Fori(0, GROUPS - 1) as g:
                for c in range(HC):
                    sp.wait_ge(taps_done, g * DVE_PER_GROUP + DVE_DONE[c])
                    load_x(g + 1, c)
                    if c % 2 == 1 and c > 2:
                        store_y(g, (c - 3) // 2)
                store_y(g, HC // 2 - 1)
            for m in range(HC // 2):
                store_y(GROUPS - 1, m)
            with sp.Fori(1, EXPERTS) as e:
                for c in range(HC):
                    load_raw(e, c, False)

        @block.scalar
        def _(act):
            act.wait_ge(pads_zero, 1)
            nc.scalar.activation(top[:, 0:PAD], x_sb[:, 0, 0, 0:PAD], ACT.Identity)
            act.wait_ge(taps_in, 16)
            act.wait_ge(bias_in, 16)

            def seed(g, c, first):
                if not first:
                    act.wait_ge(turned, ((g - 1) * HC + c + 1) * 2)
                if PE_COUNT[c]:
                    act.wait_ge(conv_mm, pe_units(g, c))
                    nc.scalar.activation(y_t[:, c, :, :], conv_ps[PE_CHUNKS.index(c) % 2], ACT.Identity,
                                         bias=bias[:, c:c + 1]).then_inc(conv_seed, 1)
                else:
                    act.wait_ge(x_in[c], (g + 1) * 16)
                    nc.scalar.activation(y_t[:, c, :, :], x_sb[:, c, :, ACT_TAP:ACT_TAP + SEQ], ACT.Identity,
                                         bias=bias[:, c:c + 1], scale=taps[:, c, ACT_TAP:ACT_TAP + 1]).then_inc(conv_seed, 1)

            def copy_out(g, c, first):
                for h in range(2):
                    act.wait_ge(turned, (g * HC + c) * 2 + h + 1)
                    if c % 2 == 0 and h == 0 and not (first and c < 4):
                        act.wait_ge(y_out[c // 2 % 2], g * 32 + c // 4 * 16)
                    nc.scalar.copy(stage[c // 2 % 2][:, 4 * h:4 * h + 4, c % 2 * P:(c % 2 + 1) * P],
                                   turn_ps[h].rearrange("p (j n) -> p j n", j=TPG // 2)).then_inc(turn_copied, 1)

            def high(e, buf, c):
                act.wait_ge(raw_in[c % RAW], (e * (HC // RAW) + (c // RAW + 1)) * 16)
                nc.scalar.copy(w_sb[:, bass.ds(buf * W_SIZE + c * H, H)], w_raw[:, c % RAW, :]).then_inc(w_hi, 1)


            for c in range(HC):
                seed(0, c, True)
                if c >= LAG:
                    copy_out(0, c - LAG, True)
            with act.Fori(1, GROUPS) as g:
                for c in range(HC):
                    seed(g, c, False)
                    copy_out(g - (c < LAG), (c - LAG) % HC, False)
            for c in range(HC):
                high(0, 0, c)
            for c in range(LAG, HC):
                copy_out(GROUPS - 1, c, False)
            act.wait_ge(ids_ready, 1)
            for c in range(HIGH_SECOND):
                high(1, 1, c)
            act.wait_ge(slots_ready, 1)

            def slot(i, k, first):
                t = i * RING + k
                act.wait_ge(ys_turned, t + 1)
                if not first:
                    act.wait_ge(gemm_done, i * RING + (k + 1 - RING))
                nc.scalar.copy(ys[:, HI, k, :, :].rearrange("p c s -> p (c s)"), turn_both).then_inc(ys_hi, 1)
                if first and k == 0:
                    for c in range(HIGH_SECOND, HC):
                        high(1, 1, c)
                if first:
                    return
                new = act.value_load(slot_first[0:1, bass.ds(t - 1, 1)], min_val=0, max_val=1)
                with act.If(new == 1):
                    e = act.value_load(slot_expert[0:1, bass.ds(t - 1, 1)], min_val=1, max_val=EXPERTS - 2)
                    act.wait_ge(gemm_done, t - 1)
                    for c in range(HC):
                        high(e + 1, (e + 1) % WBUFS, c)

            for k in range(RING):
                slot(0, k, True)
            last = act.value_load(last_round[0:1, 2:3], min_val=0, max_val=ROUNDS - 1)
            with act.Fori(1, ROUNDS) as i:
                with act.If(i < last + 1):
                    for k in range(RING):
                        slot(i, k, False)

        @block.vector
        def _(dve):
            nc.vector.memset(x_sb[:, :, :, 0:PAD], 0.0).then_inc(pads_zero, 1)
            dve.wait_ge(taps_in, 16)
            dve.wait_ge(pads_zero, 1)
            with dve.Fori(0, GROUPS) as g:
                for c, k, before in DVE_ORDER:
                    if before is None:
                        dve.wait_ge(x_in[c], (g + 1) * 16)
                        dve.wait_ge(conv_seed, g * HC + c + 1)
                    else:
                        dve.wait_ge(taps_done, g * DVE_PER_GROUP + before + 1)
                    y = y_t[:, c, :, :]
                    nc.vector.scalar_tensor_tensor(out=y, in0=x_sb[:, c, :, k:k + SEQ], scalar=taps[:, c, k:k + 1],
                                                   in1=y, op0=ALU.mult, op1=ALU.add).then_inc(taps_done, 1)

            def low(e, buf, c):
                dve.wait_ge(w_hi, e * HC + c + 1)
                nc.vector.tensor_tensor(w_sb[:, bass.ds(buf * W_SIZE + (HC + c) * H, H)], w_raw[:, c % RAW, :],
                                        w_sb[:, bass.ds(buf * W_SIZE + c * H, H)].bitcast(F32), ALU.subtract
                                        ).then_inc(w_split, 1)

            for c in range(LOW_FIRST):
                low(0, 0, c)

            steps = [0]

            def step(ins):
                steps[0] += 1
                ins.then_inc(route_step, 1)
                dve.wait_ge(route_step, steps[0])

            def per_token(a):
                return a.unsqueeze(2).to_broadcast([P, TILES, EXPERTS])

            def per_tile(a):
                return a.unsqueeze(1).to_broadcast([P, TILES, EXPERTS])

            dve.wait_ge(logit_done, GROUPS * HC)
            dve.wait_ge(const_in, 16)
            step(nc.vector.tensor_copy(logits[:, :, :], logit_ps))
            step(nc.vector.tensor_reduce(top[:, :], logits[:, :, :], AX.X, ALU.max))
            step(nc.vector.tensor_tensor(pick[:, :, :], logits[:, :, :], per_token(top[:, :]), ALU.is_equal))
            step(nc.vector.tensor_tensor(pick[:, :, :], pick[:, :, :], per_tile(cst[:, C_FIRST:C_FIRST + EXPERTS]), ALU.mult))
            step(nc.vector.tensor_reduce(top[:, :], pick[:, :, :], AX.X, ALU.max))
            step(nc.vector.tensor_scalar(top[:, :], top[:, :], 1.0, None, ALU.max))
            nc.vector.tensor_tensor(chosen[:, :, :], per_token(top[:, :]), per_tile(cst[:, C_FIRST:C_FIRST + EXPERTS]),
                                    ALU.is_equal).then_inc(chosen_ready, 1)

            dve.wait_ge(ranked, 1)
            flat = scan[:, :, :].rearrange("p e t -> p (e t)")
            step(nc.vector.tensor_tensor_scan(flat, cst[:, C_CARRY:C_CARRY + EXPERTS * TILES], total_ps, 0.0, ALU.mult, ALU.add))
            step(nc.vector.tensor_tensor(many[:, :, :], scan[:, :, TILES - 1].unsqueeze(2).to_broadcast([P, EXPERTS, TILES]),
                                         cst[:, C_SPLIT:C_SPLIT + TILES].unsqueeze(1).to_broadcast([P, EXPERTS, TILES]),
                                         ALU.is_gt))
            step(nc.vector.tensor_reduce(small[:, 2, :], many[:, :, :], AX.X, ALU.add))
            step(nc.vector.tensor_scalar(small[:, 2, :], small[:, 2, :], 1.0, None, ALU.max))
            end, start = small[:, 0, :], small[:, 3, :]
            step(nc.vector.tensor_tensor_scan(end, cst[:, C_ONES:C_ONES + EXPERTS], small[:, 2, :], 0.0, ALU.mult, ALU.add))
            step(nc.vector.tensor_tensor(start, end, small[:, 2, :], ALU.subtract))
            step(nc.vector.scalar_tensor_tensor(out=place[:, :, :], in0=start.unsqueeze(2).to_broadcast([P, EXPERTS, TILES]),
                                                scalar=float(P), in1=scan[:, :, :], op0=ALU.mult, op1=ALU.add))
            step(nc.vector.tensor_tensor(place[:, :, :].rearrange("p e t -> p (e t)"), rank_ps,
                                         place[:, :, :].rearrange("p e t -> p (e t)"), ALU.add))
            step(nc.vector.tensor_tensor(pick[:, :, :], place[:, :, :].rearrange("p e t -> p t e"), chosen[:, :, :], ALU.mult))
            step(nc.vector.tensor_reduce(pos[:, :], pick[:, :, :], AX.X, ALU.add))
            step(nc.vector.tensor_copy(pos_i[:, 0, :], pos[:, :]))
            step(nc.vector.tensor_scalar(pos_i[:, 1, :], pos_i[:, 0, :], P - 1, None, ALU.bitwise_and))
            step(nc.vector.tensor_scalar(pos_i[:, 2, :], pos_i[:, 0, :], 7, None, ALU.logical_shift_right))
            nc.vector.tensor_tensor(slot_eq, pos_i[:, 2, :].unsqueeze(2).to_broadcast([P, TILES, SLOTS]),
                                    cst[:, C_SLOT:C_SLOT + SLOTS].unsqueeze(1).to_broadcast([P, TILES, SLOTS]),
                                    ALU.is_equal).then_inc(slot_known, 1)
            dve.wait_ge(slot_known, 1)
            nc.vector.tensor_scalar(slot_hot[:, :, 0:SLOTS], slot_eq, cst[:, C_ROW:C_ROW + 1], None, ALU.mult
                                    ).then_inc(hot_ready, 1)
            for t in range(0, TILES, HOT):
                nc.vector.tensor_tensor(row_hot[:, t:t + HOT, :], pos_i[:, 1, t:t + HOT].unsqueeze(2).to_broadcast([P, HOT, P]),
                                        cst[:, C_IOTA:C_IOTA + P].unsqueeze(1).to_broadcast([P, HOT, P]), ALU.is_equal
                                        ).then_inc(row_hot_ready, 1)
            low(0, 0, LOW_FIRST)
            dve.wait_ge(ids_done, 1)
            step(nc.vector.tensor_copy(ids[:, 0:2, :].rearrange("p a s -> p (a s)"), ids_ps))
            step(nc.vector.tensor_scalar(ids[:, 2, :], ids[:, 1, :], 0.5, float(2 * TOKENS), ALU.is_lt, ALU.mult))
            step(nc.vector.scalar_tensor_tensor(out=ids[:, 3, :], in0=ids[:, 1, :], scalar=float(P), in1=ids[:, 0, :],
                                                op0=ALU.mult, op1=ALU.add))
            nc.vector.scalar_tensor_tensor(out=ids_i[:, :], in0=ids[:, 3, :], scalar=float(-P), in1=ids[:, 2, :],
                                           op0=ALU.add, op1=ALU.add).then_inc(ids_ready, 1)
            def per_slot(a, n):
                return a.unsqueeze(1).to_broadcast([P, SLOTS, n])

            def slots(n):
                return cst[:, C_SLOT:C_SLOT + SLOTS].unsqueeze(2).to_broadcast([P, SLOTS, n])

            step(nc.vector.tensor_tensor(slot_cmp[:, :, :], slots(EXPERTS), per_slot(end, EXPERTS), ALU.is_ge))
            step(nc.vector.tensor_reduce(slot_f[:, :], slot_cmp[:, :, :], AX.X, ALU.add))
            step(nc.vector.tensor_scalar(slot_expert[:, :], slot_f[:, :], float(EXPERTS - 1), None, ALU.min))
            step(nc.vector.tensor_tensor(slot_cmp[:, :, 0:EXPERTS - 2], slots(EXPERTS - 2),
                                         per_slot(start[:, 1:EXPERTS - 1], EXPERTS - 2), ALU.is_equal))
            step(nc.vector.tensor_reduce(slot_f[:, :], slot_cmp[:, :, 0:EXPERTS - 2], AX.X, ALU.add))
            step(nc.vector.tensor_copy(slot_first[:, :], slot_f[:, :]))
            step(nc.vector.tensor_copy(last_round[:, 0:1], end[:, EXPERTS - 1:EXPERTS]))
            step(nc.vector.tensor_scalar(last_round[:, 1:2], last_round[:, 0:1], -1.0, None, ALU.add))
            step(nc.vector.tensor_scalar(full_rounds[:, :], last_round[:, 0:1], RING.bit_length() - 1, None,
                                         ALU.logical_shift_right))
            nc.vector.tensor_scalar(last_round[:, 2:3], last_round[:, 1:2], RING.bit_length() - 1, None, ALU.logical_shift_right
                                    ).then_inc(slots_ready, 1)
            low(0, 0, LOW_FIRST + 1)
            dve.wait_ge(slots_ready, 1)

            def residual(i, k):
                dve.wait_ge(gemm_done, i * RING + k + 1)
                dve.wait_ge(x_got[k], (i + 1) * 16)
                nc.vector.tensor_tensor(x_row[:, k, :], out_ps[k], x_row[:, k, :], ALU.add).then_inc(res_done, 1)

            def slot(i, k, first):
                t = i * RING + k
                dve.wait_ge(ys_hi, t + 1)
                nc.vector.tensor_tensor(ys[:, LO, k, :, :].rearrange("p c s -> p (c s)"), turn_both,
                                        ys[:, HI, k, :, :].rearrange("p c s -> p (c s)").bitcast(F32), ALU.subtract
                                        ).then_inc(ys_lo, 1)
                if first and k == 0:
                    for c in range(LOW_FIRST + 2, HC):
                        low(0, 0, c)
                    for c in range(HC):
                        low(1, 1, c)
                if first:
                    return
                residual(i - 1, k)
                new = dve.value_load(slot_first[0:1, bass.ds(t - 1, 1)], min_val=0, max_val=1)
                with dve.If(new == 1):
                    e = dve.value_load(slot_expert[0:1, bass.ds(t - 1, 1)], min_val=1, max_val=EXPERTS - 2)
                    for c in range(HC):
                        low(e + 1, (e + 1) % WBUFS, c)

            for k in range(RING):
                slot(0, k, True)
            last = dve.value_load(last_round[0:1, 2:3], min_val=0, max_val=ROUNDS - 1)
            full = dve.value_load(full_rounds[0:1, 0:1], min_val=0, max_val=ROUNDS)
            with dve.Fori(1, ROUNDS) as i:
                with dve.If(i < last + 1):
                    for k in range(RING):
                        slot(i, k, False)
            residual(last, 0)
            with dve.If(last < full):
                residual(last, 1)

        @block.tensor
        def _(pe):
            pe.wait_ge(ident_in, 16)
            pe.wait_ge(router_in, 16)
            pe.wait_ge(pads_zero, 1)

            def conv(g, c, first):
                n = PE_CHUNKS.index(c)
                if first:
                    pe.wait_ge(diag_ready, 1 + DIAG[c, PE_TAPS[c][-1]])
                pe.wait_ge(x_in[c], (g + 1) * 16)
                if not (first and n < 2):
                    back = PE_CHUNKS[n - 2 if n >= 2 else N_PE - 1 - (N_PE - 1 - n) % 2]
                    pe.wait_ge(conv_seed, (g if n >= 2 else g - 1) * HC + back + 1)
                for b in range(GROUP):
                    for k in PE_TAPS[c]:
                        mm = nc.tensor.matmul(conv_ps[n % 2][:, b, :], diag[:, DIAG[c, k], :], x_sb[:, c, b, k:k + SEQ],
                                              start=(k == PE_TAPS[c][0]), stop=(k == PE_TAPS[c][-1]))
                mm.then_inc(conv_mm, 1)

            def logits_of(g, c, j):
                return nc.tensor.matmul(ps[:, 4, bass.ds((g * TPG + j) * EXPERTS, EXPERTS)],
                                        y_t[:, c, :, :].rearrange("p b s -> p (b s)")[:, j * P:(j + 1) * P], wr[:, c, :],
                                        start=(c == 0 and j == 0), stop=(c == HC - 1 and j == TPG - 1), skip_group_check=True)

            def wait_taps(g, c):
                pe.wait_ge(taps_done, g * DVE_PER_GROUP + DVE_DONE[c])

            def turn_y(g, c, first, with_logits):
                for h in range(2):
                    if not (first and c == 0):
                        pe.wait_ge(turn_copied, (g * HC + c) * 2 + h - 1)
                    for q in range(TPG // 2):
                        j = h * (TPG // 2) + q
                        tr = nc.tensor.transpose(turn_ps[h][:, q * P:(q + 1) * P],
                                                 y_t[:, c, :, :].rearrange("p b s -> p (b s)")[:, j * P:(j + 1) * P], ident)
                        if q == TPG // 2 - 1:
                            tr.then_inc(turned, 1)
                        if with_logits:
                            mm = logits_of(g, c, j)
                if with_logits:
                    mm.then_inc(logit_done, 1)

            for c in range(HC):
                if PE_COUNT[c]:
                    conv(0, c, True)
                if c >= LAG:
                    wait_taps(0, c - LAG)
                    turn_y(0, c - LAG, True, True)
            with pe.Fori(1, GROUPS) as g:
                for c in range(HC):
                    if PE_COUNT[c]:
                        conv(g, c, False)
                    wait_taps(g - (c < LAG), (c - LAG) % HC)
                    turn_y(g - (c < LAG), (c - LAG) % HC, False, True)
            for c in range(LAG, HC):
                wait_taps(GROUPS - 1, c)
                for j in range(TPG):
                    mm = logits_of(GROUPS - 1, c, j)
                mm.then_inc(logit_done, 1)
            for c in range(LAG, HC - TURN_LATE):
                turn_y(GROUPS - 1, c, False, False)

            pe.wait_ge(chosen_ready, 1)
            hot = chosen[:, :, :].rearrange("p t e -> p e t")
            pe.wait_ge(before_ready, 2)
            nc.tensor.matmul(total_ps, before[:, P:], hot, start=True, stop=True)
            nc.tensor.matmul(rank_ps, before[:, 0:P], hot, start=True, stop=True).then_inc(ranked, 1)
            for c in range(HC - TURN_LATE, HC):
                turn_y(GROUPS - 1, c, False, False)
            pe.wait_ge(hot_ready, 2)
            for t in range(TILES):
                if t % HOT == 0:
                    pe.wait_ge(row_hot_ready, t // HOT + 1)
                mm = nc.tensor.matmul(ids_ps, row_hot[:, t, :], slot_hot[:, t, :], start=(t == 0), stop=(t == TILES - 1))
            mm.then_inc(ids_done, 1)

            def turn(i, k, first):
                pe.wait_ge(y_got[k], (i + 1) * 16)
                if not first:
                    pe.wait_ge(ys_lo, i * RING + k)
                for c in range(HC):
                    tr = nc.tensor.transpose(turn_ps[c // 4][:, c % 4 * P:(c % 4 + 1) * P],
                                             y_row[:, k, c * P:(c + 1) * P], ident)
                tr.then_inc(ys_turned, 1)

            def gemm(i, k, first):
                e = pe.value_load(slot_expert[0:1, bass.ds(i * RING + k, 1)], min_val=0, max_val=EXPERTS - 1)
                pe.wait_ge(ys_lo, i * RING + k + 1)
                if not (first and k == 0):
                    pe.wait_ge(w_split, (e + 1) * HC)
                if not first:
                    pe.wait_ge(res_done, i * RING + (k + 1 - RING))
                at = (e % WBUFS) * W_SIZE
                for c in range(HC):
                    if first and k == 0:
                        pe.wait_ge(w_split, c + 1)
                    for a, b in ((HI, HI), (HI, LO), (LO, HI)):
                        for f in range(2):
                            mm = nc.tensor.matmul(out_ps[k][:, f * HALF:(f + 1) * HALF], ys[:, a, k, c, :],
                                                  w_sb[:, bass.ds(at + ((b * HC + c) * H + f * HALF), HALF)],
                                                  start=(c == 0 and (a, b) == (HI, HI)),
                                                  stop=(c == HC - 1 and (a, b) == (LO, HI)))
                mm.then_inc(gemm_done, 1)

            pe.wait_ge(slots_ready, 1)
            turn(0, 0, True)
            for k in range(RING):
                turn((k + 1) // RING, (k + 1) % RING, False)
                gemm(0, k, True)
            last = pe.value_load(last_round[0:1, 2:3], min_val=0, max_val=ROUNDS - 1)
            full = pe.value_load(full_rounds[0:1, 0:1], min_val=0, max_val=ROUNDS)
            with pe.Fori(1, ROUNDS) as i:
                with pe.If(i < last + 1):
                    turn(i, 1, False)
                    gemm(i, 0, False)
                    with pe.If(i < full):
                        turn(i + 1, 0, False)
                        gemm(i, 1, False)

        @block.gpsimd
        def _(pool):
            last_token = pool.alloc_register("last_token")
            pool.wait_ge(ident_in, 16)
            pool.wait_ge(taps_in, 16)
            for (c, k), n in DIAG.items():
                nc.gpsimd.tensor_scalar(diag[:, n, :], ident, taps[:, c, k:k + 1], None, ALU.mult).then_inc(diag_ready, 1)
            pool.wait_ge(const_in, 16)
            nc.gpsimd.tensor_tensor(before[:, 0:P], cst[:, C_BEFORE:C_BEFORE + P], cst[:, C_ONES:C_ONES + P], ALU.subtract
                                    ).then_inc(before_ready, 1)
            nc.gpsimd.tensor_copy(before[:, P:], cst[:, C_ONES:C_ONES + P]).then_inc(before_ready, 1)

            pool.wait_ge(slot_known, 1)
            nc.gpsimd.tensor_tensor(slot_hot[:, :, SLOTS:], slot_eq,
                                    cst[:, C_TILE:C_TILE + TILES].unsqueeze(2).to_broadcast([P, TILES, SLOTS]),
                                    ALU.mult).then_inc(hot_ready, 1)

            def look_up(n, t, k, nth):
                nc.gpsimd.tensor_copy(idx[:, n, k:k + 1], ids_i[:, bass.ds(t, 1)]).then_inc(idx_ready, 1)
                pool.wait_ge(idx_ready, nth)
                pool.sem_inc(dma_allowed, 1)
                return bass.IndirectOffsetOnAxis(ap=idx[:, n, k:k + 1].bitcast(U32), axis=0)

            def gather_y(i, k, first):
                t = i * RING + k
                if not first:
                    pool.wait_ge(ys_turned, t + (1 - RING))
                    pool.sem_inc(dma_allowed, 1)
                nth = t + 1 + (t - 1) if not (first and k == 0) else 1
                at = look_up(0, t, k, nth)
                nc.gpsimd.indirect_dma_start(y_row[:, k, :], None, y_dram, at, bounds_check=last_token,
                                             oob_is_err=False).then_inc(y_got[k], 16)

            def gather_x(i, k, first):
                t = i * RING + k
                if not first:
                    pool.wait_ge(row_out[k], i * 16)
                    pool.sem_inc(dma_allowed, 1)
                at = look_up(1, t, k, (t + 2) + (t + 1))
                nc.gpsimd.indirect_dma_start(x_row[:, k, :], None, x_rows, at, bounds_check=last_token,
                                             oob_is_err=False).then_inc(x_got[k], 16)

            def scatter(i, k):
                pool.wait_ge(res_done, i * RING + k + 1)
                pool.sem_inc(dma_allowed, 1)
                at = bass.IndirectOffsetOnAxis(ap=idx[:, 1, k:k + 1].bitcast(U32), axis=0)
                nc.gpsimd.indirect_dma_start(out, at, x_row[:, k, :], None, bounds_check=last_token,
                                             oob_is_err=False).then_inc(row_out[k], 16)

            pool.reg_mov(last_token, TOKENS - 1)
            for n in range(2):
                pool.wait_ge(y_out[n], 16 * GROUPS * HC // 4)
            pool.wait_ge(ids_ready, 1)
            gather_y(0, 0, True)
            gather_y(0, 1, True)
            gather_x(0, 0, True)
            gather_y(1, 0, False)
            gather_x(0, 1, True)
            pool.wait_ge(slots_ready, 1)
            last = pool.value_load(last_round[0:1, 2:3], min_val=0, max_val=ROUNDS - 1)
            full = pool.value_load(full_rounds[0:1, 0:1], min_val=0, max_val=ROUNDS)
            with pool.Fori(1, ROUNDS) as i:
                with pool.If(i < last + 1):
                    for k in range(RING):
                        gather_y(i + (k + 1) // RING, (k + 1) % RING, False)
                        scatter(i - 1, k)
                        gather_x(i, k, False)
            scatter(last, 0)
            with pool.If(last < full):
                scatter(last, 1)
            pool.wait_ge(row_out[0], (last + 1) * 16)
            pool.wait_ge(row_out[1], full * 16)
def kernel(x, cond_2048, L0_cond_b, L0_ffn_w_router, L0_ffn_w_experts):
    import numpy as _np
    import concourse.bacc as _bacc
    from concourse import mybir as _mybir
    from concourse.bass_utils import run_bass_kernel_spmd as _run

    x = _np.asarray(x)
    arrays = {
        "x_t": x.reshape(GROUPS, GROUP, SEQ, HC, P).transpose(0, 3, 4, 1, 2),
        "x_rows": x.reshape(TOKENS, H),
        "conv_w": _np.asarray(cond_2048).reshape(TAPS, HC, P).transpose(2, 1, 0),
        "conv_b": _np.asarray(L0_cond_b).reshape(HC, P).transpose(1, 0),
        "router": _np.asarray(L0_ffn_w_router).reshape(EXPERTS, HC, P).transpose(2, 1, 0),
        "experts": _np.asarray(L0_ffn_w_experts).reshape(EXPERTS, H, HC, P).transpose(0, 3, 2, 1),
        "consts": shape_constants(),
    }
    arrays = {k: _np.ascontiguousarray(v) for k, v in arrays.items()}
    nc = _bacc.Bacc("TRN2", target_bir_lowering=False, num_devices=1)
    args = [nc.dram_tensor(k, v.shape, _mybir.dt.from_np(v.dtype), kind="ExternalInput").ap() for k, v in arrays.items()]
    out = nc.dram_tensor("out", (TOKENS, H), _mybir.dt.float32, kind="ExternalOutput").ap()
    build(nc, *args, out)
    r = _run(nc, [arrays], core_ids=[0])
    return r.results[0]["out"].reshape(BATCH, SEQ, H)
```
